# Optimizing a Trainium2 kernel written in Bass

```python
import numpy as np
import jax
import jax.numpy as jnp

def _softmax(x, axis=-1):
    return jax.nn.softmax(x, axis=axis)

def _gelu(x):
    return jax.nn.gelu(x, approximate=True)

def _silu(x):
    return jax.nn.silu(x)

def _sigmoid(x):
    return jax.nn.sigmoid(x)

def _layernorm(x, axis=-1, eps=1e-05):
    m = jnp.mean(x, axis=axis, keepdims=True)
    v = jnp.var(x, axis=axis, keepdims=True)
    return (x - m) / jnp.sqrt(v + eps)

def _scatter_add(tgt, idx, src, axis=0):
    return tgt.at[idx].add(src)

def _segment_sum(src, seg, n):
    return jax.ops.segment_sum(src, seg, n)
kernel_name = 'mk_adaln_ffn_d1_seqx_r4_3c47a5'

def setup_inputs(seed: int=0):
    np.random.seed(seed)
    _w = jnp.asarray

    def _rec_inputs():
        import jax
        import jax.numpy as jnp
        _rk = jax.random.key(seed)
        x = -7.109e-05 + 0.9999 * jax.random.normal(jax.random.fold_in(_rk, 1), (64, 64, 1024), jnp.float32)
        _lenS = 64 - jax.random.randint(jax.random.fold_in(_rk, 7), (64,), 0, max(1, 64 // 4) + 1, jnp.int32)
        _lenS2 = 64 - jax.random.randint(jax.random.fold_in(_rk, 8), (64,), 0, max(1, 64 // 4) + 1, jnp.int32)
        itok_B_0_15 = jax.random.randint(jax.random.fold_in(_rk, 11), (64,), 0, 16, jnp.int32)
        return (x, itok_B_0_15)
    x, itok_B_0_15 = _rec_inputs()

    def _L0_cond_setup():
        import jax, jax.numpy as jnp
        import numpy as np
        NUM_CONDITIONS = 16
        IN_CH = 64
        OUT_CH = 64
        B = 64
        T = 1024
        key = jax.random.key(seed)
        k_x, k_w, k_c = jax.random.split(key, 3)
        x = jax.random.normal(k_x, (B, IN_CH, T), dtype=jnp.float32)
        bound = float(np.sqrt(6.0 / IN_CH))
        weights = jax.random.uniform(k_w, (NUM_CONDITIONS, IN_CH, OUT_CH), dtype=jnp.float32, minval=-bound, maxval=bound)
        condition = jax.random.randint(k_c, (B,), 0, NUM_CONDITIONS, dtype=jnp.int64)
        return {'x': x, 'weights': weights, 'condition': condition}
    _L0_cond_all = _L0_cond_setup()
    _L0_cond_in = {k: v for k, v in _L0_cond_all.items() if k in ('weights',)}
    del _L0_cond_all

    def _L0_ffn_setup():
        import jax, jax.numpy as jnp
        import numpy as np
        import math
        B, S, IN, OUT = (4, 512, 1024, 1024)
        E, R, K = (8, 64, 128)
        SCALE = 64.0 / 64.0
        MULTIPLIER = 1.0
        key = jax.random.key(seed)
        ks = jax.random.split(key, 6)
        return {'x': jax.random.normal(ks[0], (B, S, IN), jnp.float32), 'W_org': jax.random.normal(ks[1], (OUT, IN), jnp.float32) * 0.02, 'lora_down': jax.random.normal(ks[2], (E, IN, R), jnp.float32) * 0.02, 'lora_up': jax.random.normal(ks[3], (E, R, OUT), jnp.float32) * 0.02, 'lora_keys': jax.random.normal(ks[4], (E, K), jnp.float32), 'Wq': jax.random.normal(ks[5], (K, IN), jnp.float32) * 0.02}
    _L0_ffn_all = _L0_ffn_setup()
    _L0_ffn_in = {k: v for k, v in _L0_ffn_all.items() if k in ('W_org', 'lora_down', 'lora_up', 'lora_keys', 'Wq')}
    del _L0_ffn_all
    return {'x': x, 'itok_B_0_15': itok_B_0_15, 'L0_cond_weights': _L0_cond_in['weights'], 'L0_ffn_W_org': _L0_ffn_in['W_org'], 'L0_ffn_lora_down': _L0_ffn_in['lora_down'], 'L0_ffn_lora_up': _L0_ffn_in['lora_up'], 'L0_ffn_lora_keys': _L0_ffn_in['lora_keys'], 'L0_ffn_Wq': _L0_ffn_in['Wq']}

def reference(x, itok_B_0_15, L0_cond_weights, L0_ffn_W_org, L0_ffn_lora_down, L0_ffn_lora_up, L0_ffn_lora_keys, L0_ffn_Wq):
    import jax
    import jax.numpy as jnp

    def _L0_cond_ref(x, weights, condition):
        import jax, jax.numpy as jnp
        import numpy as np
        NUM_CONDITIONS = 16
        IN_CH = 64
        OUT_CH = 64
        B = 64
        T = 1024
        W = weights[condition]
        return jnp.einsum('bct,bcd->bdt', x, W)

    def _L0_ffn_ref(x, W_org, lora_down, lora_up, lora_keys, Wq):
        import jax, jax.numpy as jnp
        import numpy as np
        import math
        B, S, IN, OUT = (4, 512, 1024, 1024)
        E, R, K = (8, 64, 128)
        SCALE = 64.0 / 64.0
        MULTIPLIER = 1.0
        base = jnp.einsum('bsi,oi->bso', x, W_org)
        q = jnp.einsum('bi,ki->bk', x.mean(axis=1), Wq)
        scores = jnp.einsum('bk,ek->be', q, lora_keys) / math.sqrt(K)
        coeffs = jax.nn.softmax(scores, axis=-1)
        h = jnp.einsum('bsi,eir->bser', x, lora_down)
        delta = jnp.einsum('be,bser,ero->bso', coeffs, h, lora_up)
        return base + delta * (SCALE * MULTIPLIER)
    x = x + _L0_ffn_ref(_L0_cond_ref(x, L0_cond_weights, itok_B_0_15), L0_ffn_W_org, L0_ffn_lora_down, L0_ffn_lora_up, L0_ffn_lora_keys, L0_ffn_Wq)
    return x

_drawn_inputs = setup_inputs


def setup_inputs(seed=0):
    import zlib

    import numpy as np

    out = dict(_drawn_inputs(seed))
    spreads = {}
    factors = {'L0_ffn_lora_keys': 8.0, 'L0_ffn_Wq': 8.0}
    for name, (base, spread) in spreads.items():
        noise = np.random.default_rng([zlib.crc32(name.encode()), seed]).standard_normal(out[name].shape)
        drawn = base * np.exp(spread * noise) if base else spread * noise
        out[name] = jnp.asarray(drawn.astype(out[name].dtype))
    for name, factor in factors.items():
        out[name] = (out[name] * factor).astype(out[name].dtype)
    return out
```

```python
from contextlib import ExitStack

import concourse.bass as bass
from concourse import mybir

P = 128
F32 = mybir.dt.float32
F32R = mybir.dt.float32r
I32 = mybir.dt.int32
ALU = mybir.AluOpType
ACT = mybir.ActivationFunctionType
AX = mybir.AxisListType


def adaln_ffn(
    nc: bass.Bass,
    x: bass.AP,
    cond: bass.AP,
    cond_w: bass.AP,
    w_org: bass.AP,
    lora_down: bass.AP,
    lora_up: bass.AP,
    lora_keys: bass.AP,
    wq: bass.AP,
    out: bass.AP,
):
    B, C, IN = x.shape
    NCOND = cond_w.shape[0]
    OUT = w_org.shape[0]
    E, _, R = lora_down.shape
    K = wq.shape[0]
    ER = E * R
    BT = P // C
    T = B // BT
    KC = IN // P
    EC = ER // P
    OC = OUT // P
    BANK = 512
    NH = OUT // BANK
    YR = 2
    YC = KC // YR
    HK = KC // 2
    assert BT == 2 and NH == 2 and ER == BANK and YC * 2 * P == 2 * BANK and K == P and T % 2 == 0

    DP = KC * ER // IN
    EP = E // DP
    assert DP == EC == OC // 2
    x_v = x.rearrange("(t b) c s -> t (b c) s", b=BT)
    out_v = out.rearrange("(t b) c s -> t (b c) s", b=BT)
    cond_v = cond.rearrange("(a b) -> a b", a=1)
    down_v = lora_down.rearrange("(n a) (p k) r -> n p a k r", n=DP, k=KC)
    up_v = lora_up.rearrange("(m a) r o -> m (a r) o", m=EC)
    org_v = w_org.rearrange("(c p) i -> c p i", p=P)

    pieces = [("down", n) for n in range(DP)] + [("wq", 0)]
    pieces += [("org", n) for n in range(OC)] + [("up", n) for n in range(EC)]
    place = {piece: n for n, piece in enumerate(pieces)}
    RING = 7

    with ExitStack() as ctx:
        def sb(name, shape, dt=F32):
            return ctx.enter_context(nc.sbuf_tensor(name, shape, dt))

        def psum(name, shape):
            return ctx.enter_context(nc.psum_tensor(name, shape, F32))

        def sem(name):
            return ctx.enter_context(nc.semaphore(name))

        org_t = [sb(f"org_t_{s}", [P, KC, OUT], F32R) for s in "hl"]
        down = [sb(f"down_{s}", [P, KC, ER], F32R) for s in "hl"]
        up = [sb(f"up_{s}", [P, EC, OUT], F32R) for s in "hl"]
        gate = sb("gate", [P, E, KC])
        stage_sb = sb("stage_sb", [P, RING - 2, IN])
        cond_sb = sb("cond_sb", [1, B], I32)
        x_sb = sb("x_sb", [P, 2, IN])
        cw_sb = sb("cw_sb", [P, 2, BT, C])
        xs = [sb(f"x_{s}", [P, KC, P], F32R) for s in "hl"]
        cws = sb("cws", [P, 2, BT * C], F32R)
        y_part = sb("y_part", [P, YC, P])
        y_full = sb("y_full", [P, YR, YC, P])
        y = [sb(f"y_{s}", [P, 2, KC, P], F32R) for s in "hl"]
        g_sb = sb("g_sb", [P, ER])
        gt = [sb(f"gt_{s}", [P, EC, P], F32R) for s in "hl"]
        out_sb = sb("out_sb", [P, 2, OUT])
        stage = [stage_sb[:, n, :] for n in range(RING - 2)] + [out_sb[:, n, :] for n in range(2)]
        ysum = sb("ysum", [P, KC, BT])
        yg = sb("yg", [P, BT, E, KC])
        z = sb("z", [P, BT * E])
        zs = sb("zs", [P, 2, BT * E], F32R)
        ssb = sb("ssb", [P, BT, E])
        smax = sb("smax", [P, BT])
        sdiff = sb("sdiff", [P, BT, E])
        sexp = sb("sexp", [P, BT, E])
        ssum = sb("ssum", [P, BT])
        srec = sb("srec", [P, BT])
        coef = sb("coef", [P, E])
        ident = sb("ident", [P, P])
        ones = sb("ones", [P, P])
        ones_r = sb("ones_r", [P, P], F32R)
        keys_sb = sb("keys_sb", [E, K])
        keys_t = sb("keys_t", [K, E])

        y_ps = psum("y_ps", [P, YC, 2, P])
        h_ps = psum("h_ps", [P, ER])
        gt_ps = psum("gt_ps", [P, BANK])
        o_ps = psum("o_ps", [P, NH, BANK])
        s_ps = psum("s_ps", [P, BANK])
        t_ps = psum("t_ps", [P, BANK])
        scores = s_ps[:, 0:2 * BT * E]
        keys_ps = s_ps[:, 64:64 + E]
        gate_ps = s_ps[:, 128:128 + KC * E].rearrange("p (k e) -> p k e", e=E)
        turn_ps = [gt_ps[:, :], t_ps[:, :]] + [
            y_ps[:, j * YC // 2:(j + 1) * YC // 2, :, :].rearrange("p k h n -> p (k h n)") for j in range(2)]
        TB = len(turn_ps)

        def down_piece(s, n):
            return down[s][:, :, n * EP * R:(n + 1) * EP * R].rearrange("p k (a r) -> p a k r", a=EP)

        def chunk_cols(ap, ks):
            return ap.rearrange("p (i k) -> p k i", k=KC)[:, ks, :]

        cond_loaded = sem("cond_loaded")
        keys_loaded = sem("keys_loaded")
        piece_loaded = [sem(f"piece_loaded_{n}") for n in range(len(pieces))]
        x_loaded = [sem(f"x_loaded_{p}") for p in range(2)]
        cw_loaded = [sem(f"cw_loaded_{p}") for p in range(2)]
        stored = [sem(f"stored_{p}") for p in range(2)]
        ident_zero = sem("ident_zero")
        ident_ready = sem("ident_ready")
        ones_ready = sem("ones_ready")
        keys_turned = sem("keys_turned")
        keys_ready = sem("keys_ready")
        gate_done = sem("gate_done")
        gate_ready = sem("gate_ready")
        org_turned = sem("org_turned")
        org_hi = sem("org_hi")
        org_lo = sem("org_lo")
        down_hi = sem("down_hi")
        down_lo = [sem(f"down_lo_{n}") for n in range(DP)]
        up_hi = sem("up_hi")
        up_lo = [sem(f"up_lo_{n}") for n in range(EC)]
        ones_copied = sem("ones_copied")
        x_hi = sem("x_hi")
        x_lo = sem("x_lo")
        cw_hi = sem("cw_hi")
        cw_lo = sem("cw_lo")
        cw_zeroed = sem("cw_zeroed")
        y_done = sem("y_done")
        y_copied = sem("y_copied")
        y_added = sem("y_added")
        y_hi = sem("y_hi")
        y_lo = sem("y_lo")
        y_summed = sem("y_summed")
        yg_ready = sem("yg_ready")
        z_ready = sem("z_ready")
        z_hi = sem("z_hi")
        z_lo = sem("z_lo")
        scores_ready = sem("scores_ready")
        scores_done = sem("scores_done")
        smax_ready = sem("smax_ready")
        sdiff_ready = sem("sdiff_ready")
        sexp_ready = sem("sexp_ready")
        ssum_ready = sem("ssum_ready")
        srec_ready = sem("srec_ready")
        coef_ready = sem("coef_ready")
        h_done = sem("h_done")
        g_ready = sem("g_ready")
        g_turned = sem("g_turned")
        gt_hi = sem("gt_hi")
        gt_lo = sem("gt_lo")
        o_done = sem("o_done")
        out_ready = sem("out_ready")

        block = ctx.enter_context(nc.Block())

        @block.sync
        def _(sp):
            def load_x(t, p):
                sp.dma_start(x_sb[:, p, :], x_v[t, :, :]).then_inc(x_loaded[p], 16)

            def load_cw(t, p):
                for b in range(BT):
                    which = sp.value_load(cond_sb[0:1, bass.ds(BT * t + b, 1)], min_val=0, max_val=NCOND - 1)
                    sp.dma_start(cw_sb[b * C:(b + 1) * C, p, b, :], cond_w[which, :, :]).then_inc(cw_loaded[p], 16)

            def load_piece(kind, n):
                at = place[kind, n]
                slot = stage[at % RING]
                if at >= RING:
                    was, m = pieces[at - RING]
                    if was == "down":
                        sp.wait_ge(down_lo[m], 1)
                    elif was == "wq":
                        sp.wait_ge(gate_done, 1)
                    elif was == "org":
                        sp.wait_ge(org_turned, 2 * (m + 1))
                    else:
                        sp.wait_ge(up_lo[m], 1)
                if kind == "down":
                    sp.dma_start(slot.rearrange("p (a k r) -> p a k r", a=EP, k=KC),
                                 down_v[n]).then_inc(piece_loaded[at], 16)
                elif kind == "wq":
                    sp.dma_start(slot, wq).then_inc(piece_loaded[at], 16)
                elif kind == "org":
                    sp.dma_start(slot, org_v[n]).then_inc(piece_loaded[at], 16)
                else:
                    sp.dma_start(slot, up_v[n]).then_inc(piece_loaded[at], 16)

            def tile(t, p, first=False, last=False):
                if not first and not last:
                    sp.wait_ge(out_ready, 2 * t)
                    load_x(t + 1, 1 - p)
                    load_cw(t + 1, 1 - p)
                for h in range(NH):
                    sp.wait_ge(out_ready, 2 * t + h + 1)
                    sp.dma_start(out_v[t, :, h * BANK:(h + 1) * BANK],
                                 out_sb[:, p, h * BANK:(h + 1) * BANK]).then_inc(stored[p], 16)

            sp.dma_start(cond_sb[:, :], cond_v).then_inc(cond_loaded, 16)
            load_x(0, 0)
            for kind, n in pieces[0:1]:
                load_piece(kind, n)
            sp.wait_ge(cond_loaded, 16)
            sp.wait_ge(cw_zeroed, 1)
            load_cw(0, 0)
            for kind, n in pieces[1:place["up", 0]]:
                load_piece(kind, n)
            load_x(1, 1)
            load_cw(1, 1)
            for kind, n in pieces[place["up", 0]:]:
                load_piece(kind, n)
            tile(0, 0, first=True)
            with sp.Fori(0, T // 2 - 1) as i:
                for u in range(2):
                    tile(2 * i + (1 + u), (1 + u) % 2)
            tile(T - 1, 1, last=True)
            for p in range(2):
                sp.wait_ge(stored[p], 16 * NH * (T // 2))

        @block.gpsimd
        def _(pool):
            pool.memset(cw_sb[:, :, :, :], 0.0).then_inc(cw_zeroed, 1)
            pool.memset(ident[:, :], 0.0).then_inc(ident_zero, 1)
            pool.memset(ones[:, :], 1.0).then_inc(ones_ready, 1)
            pool.wait_ge(ident_zero, 1)
            pool.affine_select(out=ident[:, :], in_=ident[:, :], compare_op=ALU.not_equal, fill=1.0,
                               base=0, pattern=[[-1, P]], channel_multiplier=1).then_inc(ident_ready, 1)

            for n in range(0, DP, 2):
                at = place["down", n]
                pool.wait_ge(piece_loaded[at], 16)
                pool.wait_ge(down_hi, n + 1)
                pool.tensor_tensor(down_piece(1, n),
                                   stage[at % RING].rearrange("p (a k r) -> p a k r", a=EP, k=KC),
                                   down_piece(0, n), ALU.subtract).then_inc(down_lo[n], 1)
            for n in range(0, EC, 2):
                at = place["up", n]
                pool.wait_ge(piece_loaded[at], 16)
                pool.wait_ge(up_hi, n + 1)
                pool.tensor_tensor(up[1][:, n, :], stage[at % RING], up[0][:, n, :],
                                   ALU.subtract).then_inc(up_lo[n], 1)

        @block.scalar
        def _(act):
            act.dma_start(keys_sb[:, :], lora_keys).then_inc(keys_loaded, 16)

            def split_x(t, p, n):
                act.wait_ge(x_loaded[p], 16 * (n + 1))
                for c in range(YR):
                    ks = slice(c * YC, (c + 1) * YC)
                    nc.scalar.activation(xs[0][:, ks, :], chunk_cols(x_sb[:, p, :], ks), ACT.Copy).then_inc(x_hi, 1)
                act.wait_ge(cw_loaded[p], 16 * BT * (n + 1))
                nc.scalar.activation(cws[:, 0, :], cw_sb[:, p, :, :].rearrange("p b d -> p (b d)"),
                                     ACT.Copy).then_inc(cw_hi, 1)

            def copy_y(t, r):
                act.wait_ge(y_done, YR * t + r + 1)
                nc.scalar.activation(y_part[:, :, :], y_ps[:, :, 1, :], ACT.Copy).then_inc(y_copied, 1)

            def split_y(t, p, r):
                act.wait_ge(y_added, YR * t + r + 1)
                nc.scalar.activation(y[0][:, p, r * YC:(r + 1) * YC, :], y_full[:, r, :, :],
                                     ACT.Copy).then_inc(y_hi, 1)

            def split_z(t):
                act.wait_ge(z_ready, t + 1)
                nc.scalar.activation(zs[:, 0, :], z[:, :], ACT.Copy).then_inc(z_hi, 1)

            def exps(t):
                act.wait_ge(sdiff_ready, t + 1)
                nc.scalar.activation(sexp[:, :, :], sdiff[:, :, :], ACT.Exp,
                                     scale=1.0 / (C * float(K) ** 0.5)).then_inc(sexp_ready, 1)

            def split_g(t):
                act.wait_ge(g_turned, t + 1)
                nc.scalar.activation(gt[0][:, :, :], gt_ps[:, :].rearrange("p (m n) -> p m n", m=EC),
                                     ACT.Copy).then_inc(gt_hi, 1)

            def split_down(n):
                at = place["down", n]
                act.wait_ge(piece_loaded[at], 16)
                nc.scalar.activation(down_piece(0, n),
                                     stage[at % RING].rearrange("p (a k r) -> p a k r", a=EP, k=KC),
                                     ACT.Copy).then_inc(down_hi, 1)

            def split_org(n):
                for j in range(2):
                    act.wait_ge(org_turned, 2 * n + j + 1)
                    nc.scalar.activation(org_t[0][:, j * HK:(j + 1) * HK, n * P:(n + 1) * P],
                                         turn_ps[(2 * n + j) % TB].rearrange("p (k n) -> p k n", k=HK),
                                         ACT.Copy).then_inc(org_hi, 1)

            def split_up(n):
                at = place["up", n]
                act.wait_ge(piece_loaded[at], 16)
                nc.scalar.activation(up[0][:, n, :], stage[at % RING], ACT.Copy).then_inc(up_hi, 1)

            def tile(t, p, n, last=False):
                if not last:
                    split_x(t + 1, 1 - p, n)
                split_g(t)
                if not last:
                    for r in range(YR):
                        copy_y(t + 1, r)
                        split_y(t + 1, 1 - p, r)
                    split_z(t + 1)
                    exps(t + 1)

            split_x(0, 0, 0)
            split_down(0)
            copy_y(0, 0)
            split_down(1)
            split_y(0, 0, 0)
            split_down(2)
            copy_y(0, 1)
            split_down(3)
            split_y(0, 0, 1)
            act.wait_ge(ones_ready, 1)
            nc.scalar.activation(ones_r[:, :], ones[:, :], ACT.Copy).then_inc(ones_copied, 1)
            split_z(0)
            split_org(0)
            split_org(1)
            exps(0)
            for n in range(2, OC):
                split_org(n)
            split_x(1, 1, 0)
            split_g(0)
            split_up(0)
            split_up(1)
            copy_y(1, 0)
            split_y(1, 1, 0)
            split_up(2)
            copy_y(1, 1)
            split_y(1, 1, 1)
            split_up(3)
            split_z(1)
            exps(1)
            with act.Fori(0, T // 2 - 1) as i:
                for u in range(2):
                    tile(2 * i + (1 + u), (1 + u) % 2, i + 1)
            tile(T - 1, 1, T // 2 - 1, last=True)

        @block.vector
        def _(dve):
            def split_x(t, p, n):
                dve.wait_ge(x_loaded[p], 16 * (n + 1))
                for c in range(YR):
                    ks = slice(c * YC, (c + 1) * YC)
                    dve.wait_ge(x_hi, 2 * t + c + 1)
                    nc.vector.tensor_tensor(xs[1][:, ks, :], chunk_cols(x_sb[:, p, :], ks), xs[0][:, ks, :],
                                            ALU.subtract).then_inc(x_lo, 1)
                dve.wait_ge(cw_loaded[p], 16 * BT * (n + 1))
                dve.wait_ge(cw_hi, t + 1)
                nc.vector.tensor_tensor(cws[:, 1, :], cw_sb[:, p, :, :].rearrange("p b d -> p (b d)"),
                                        cws[:, 0, :], ALU.subtract).then_inc(cw_lo, 1)

            def split_y(t, p, r):
                n = YR * t + r + 1
                chunks = slice(r * YC, (r + 1) * YC)
                dve.wait_ge(y_copied, n)
                nc.vector.tensor_tensor(y_full[:, r, :, :], y_ps[:, :, 0, :], y_part[:, :, :],
                                        ALU.add).then_inc(y_added, 1)
                dve.wait_ge(y_added, n)
                nc.vector.tensor_reduce(ysum[:, chunks, :],
                                        y_full[:, r, :, :].rearrange("p k (b d) -> p k b d", b=BT),
                                        AX.X, ALU.add).then_inc(y_summed, 1)
                dve.wait_ge(y_hi, n)
                nc.vector.tensor_tensor(y[1][:, p, chunks, :], y_full[:, r, :, :], y[0][:, p, chunks, :],
                                        ALU.subtract).then_inc(y_lo, 1)

            def gate_sums(t):
                dve.wait_ge(y_summed, YR * t + YR)
                nc.vector.tensor_tensor(yg[:, :, :, :],
                                        ysum[:, :, :].rearrange("p k b -> p b k").unsqueeze(2).to_broadcast([P, BT, E, KC]),
                                        gate[:, :, :].unsqueeze(1).to_broadcast([P, BT, E, KC]),
                                        ALU.mult).then_inc(yg_ready, 1)
                dve.wait_ge(yg_ready, t + 1)
                nc.vector.tensor_reduce(z[:, :].rearrange("p (b e) -> p b e", b=BT), yg[:, :, :, :], AX.X,
                                        ALU.add).then_inc(z_ready, 1)

            def split_z(t):
                dve.wait_ge(z_hi, t + 1)
                nc.vector.tensor_tensor(zs[:, 1, :], z[:, :], zs[:, 0, :], ALU.subtract).then_inc(z_lo, 1)

            def softmax(t):
                dve.wait_ge(scores_done, t + 1)
                nc.vector.tensor_reduce(ssb[:, :, :].rearrange("p b e -> p (b e)"),
                                        scores.rearrange("p (h n) -> p n h", h=2), AX.X,
                                        ALU.add).then_inc(scores_ready, 1)
                dve.wait_ge(scores_ready, t + 1)
                nc.vector.tensor_reduce(smax[:, :], ssb[:, :, :], AX.X, ALU.max).then_inc(smax_ready, 1)
                dve.wait_ge(smax_ready, t + 1)
                nc.vector.tensor_tensor(sdiff[:, :, :], ssb[:, :, :],
                                        smax[:, :].unsqueeze(2).to_broadcast([P, BT, E]),
                                        ALU.subtract).then_inc(sdiff_ready, 1)
                dve.wait_ge(sexp_ready, t + 1)
                nc.vector.tensor_reduce(ssum[:, :], sexp[:, :, :], AX.X, ALU.add).then_inc(ssum_ready, 1)
                dve.wait_ge(ssum_ready, t + 1)
                nc.vector.reciprocal(srec[:, :], ssum[:, :]).then_inc(srec_ready, 1)
                dve.wait_ge(srec_ready, t + 1)
                for b in range(BT):
                    rows = slice(b * C, (b + 1) * C)
                    nc.vector.tensor_scalar(coef[rows, :], sexp[rows, b, :], srec[rows, b:b + 1], None,
                                            ALU.mult).then_inc(coef_ready, 1)

            def scale_h(t):
                dve.wait_ge(coef_ready, 2 * t + 2)
                dve.wait_ge(h_done, t + 1)
                nc.vector.tensor_tensor(g_sb[:, :].rearrange("p (e r) -> p e r", e=E),
                                        h_ps[:, :].rearrange("p (e r) -> p e r", e=E),
                                        coef[:, :].unsqueeze(2).to_broadcast([P, E, R]),
                                        ALU.mult).then_inc(g_ready, 1)

            def split_g(t):
                dve.wait_ge(gt_hi, t + 1)
                nc.vector.tensor_tensor(gt[1][:, :, :], gt_ps[:, :].rearrange("p (m n) -> p m n", m=EC),
                                        gt[0][:, :, :], ALU.subtract).then_inc(gt_lo, 1)

            def add_x(t, p, h):
                cols = slice(h * BANK, (h + 1) * BANK)
                dve.wait_ge(o_done, 2 * t + h + 1)
                nc.vector.tensor_tensor(out_sb[:, p, cols], o_ps[:, h, :], x_sb[:, p, cols],
                                        ALU.add).then_inc(out_ready, 1)

            def split_down(n):
                at = place["down", n]
                dve.wait_ge(piece_loaded[at], 16)
                dve.wait_ge(down_hi, n + 1)
                nc.vector.tensor_tensor(down_piece(1, n),
                                        stage[at % RING].rearrange("p (a k r) -> p a k r", a=EP, k=KC),
                                        down_piece(0, n), ALU.subtract).then_inc(down_lo[n], 1)

            def split_org(n):
                for j in range(2):
                    dve.wait_ge(org_hi, 2 * n + j + 1)
                    dst = slice(j * HK, (j + 1) * HK), slice(n * P, (n + 1) * P)
                    nc.vector.tensor_tensor(org_t[1][:, dst[0], dst[1]],
                                            turn_ps[(2 * n + j) % TB].rearrange("p (k n) -> p k n", k=HK),
                                            org_t[0][:, dst[0], dst[1]], ALU.subtract).then_inc(org_lo, 1)

            def split_up(n):
                at = place["up", n]
                dve.wait_ge(piece_loaded[at], 16)
                dve.wait_ge(up_hi, n + 1)
                nc.vector.tensor_tensor(up[1][:, n, :], stage[at % RING], up[0][:, n, :],
                                        ALU.subtract).then_inc(up_lo[n], 1)

            def tile(t, p, n, last=False, free=None):
                scale_h(t)
                if not last:
                    split_x(t + 1, 1 - p, n)
                split_g(t)
                if free is not None:
                    dve.wait_ge(stored[p], 16 * NH * free)
                add_x(t, p, 0)
                if not last:
                    for r in range(YR):
                        split_y(t + 1, 1 - p, r)
                    gate_sums(t + 1)
                    split_z(t + 1)
                add_x(t, p, 1)
                if not last:
                    softmax(t + 1)

            dve.wait_ge(keys_turned, 1)
            nc.vector.tensor_copy(keys_t[:, :], keys_ps).then_inc(keys_ready, 1)
            split_x(0, 0, 0)
            split_y(0, 0, 0)
            split_down(1)
            split_y(0, 0, 1)
            split_down(3)
            dve.wait_ge(gate_done, 1)
            nc.vector.tensor_copy(gate[:, :, :].rearrange("p e k -> p k e"), gate_ps).then_inc(gate_ready, 1)
            dve.wait_ge(gate_ready, 1)
            gate_sums(0)
            split_z(0)
            split_org(0)
            split_org(1)
            softmax(0)
            for n in range(2, OC):
                split_org(n)
                if n == OC // 2 - 1:
                    scale_h(0)
            split_x(1, 1, 0)
            split_g(0)
            split_y(1, 1, 0)
            split_up(1)
            split_y(1, 1, 1)
            split_up(3)
            gate_sums(1)
            split_z(1)
            add_x(0, 0, 0)
            add_x(0, 0, 1)
            softmax(1)
            tile(1, 1, 1)
            with dve.Fori(0, T // 2 - 1 - 1) as i:
                for u in range(2):
                    tile(2 * i + (2 + u), u, i + 1 + u, free=i + 1)
            tile(T - 2, 0, T // 2 - 1, free=T // 2 - 1)
            tile(T - 1, 1, T // 2, last=True, free=T // 2 - 1)

        @block.tensor
        def _(pe):
            PASSES = ((0, 0), (1, 0), (0, 1))

            def make_y(t, r):
                pe.wait_ge(x_hi, 2 * t + r + 1)
                pe.wait_ge(x_lo, 2 * t + r + 1)
                if r == 0:
                    pe.wait_ge(cw_hi, t + 1)
                    pe.wait_ge(cw_lo, t + 1)
                for k in range(YC):
                    for s in range(2):
                        mm = nc.tensor.matmul(y_ps[:, k, :, :].rearrange("p h n -> p (h n)"),
                                              xs[s][:, r * YC + k, :],
                                              cws[:, :, :].rearrange("p h n -> p (h n)"),
                                              start=(k % 2 == 0 and s == 0), stop=(k % 2 == 1 and s == 1),
                                              skip_group_check=True)
                mm.then_inc(y_done, 1)

            def make_h(t, p, ks):
                for k in ks:
                    if k % YC == 0:
                        r = k // YC
                        pe.wait_ge(y_hi, YR * t + r + 1)
                        pe.wait_ge(y_lo, YR * t + r + 1)
                    for q, (s, m) in enumerate(PASSES):
                        mm = nc.tensor.matmul(h_ps[:, :], y[s][:, p, k, :], down[m][:, k, :],
                                              start=(k == 0 and q == 0), stop=(k == KC - 1 and q == 2))
                if ks[-1] == KC - 1:
                    mm.then_inc(h_done, 1)

            def base(t, p, h, ks):
                for k in ks:
                    for q, (s, m) in enumerate(PASSES):
                        nc.tensor.matmul(o_ps[:, h, :], y[s][:, p, k, :],
                                         org_t[m][:, k, h * BANK:(h + 1) * BANK],
                                         start=(k == 0 and q == 0), stop=False)

            def turn_g(t):
                pe.wait_ge(g_ready, t + 1)
                for m in range(EC):
                    mm = nc.tensor.transpose(gt_ps[:, m * P:(m + 1) * P], g_sb[:, m * P:(m + 1) * P], ident[:, :])
                mm.then_inc(g_turned, 1)

            def add_lora(t, h, first=False):
                pe.wait_ge(gt_hi, t + 1)
                pe.wait_ge(gt_lo, t + 1)
                for e in range(EC):
                    if first:
                        pe.wait_ge(up_hi, e + 1)
                        pe.wait_ge(up_lo[e], 1)
                    for q, (s, m) in enumerate(PASSES):
                        mm = nc.tensor.matmul(o_ps[:, h, :], gt[s][:, e, :],
                                              up[m][:, e, h * BANK:(h + 1) * BANK],
                                              start=False, stop=(e == EC - 1 and q == 2))
                mm.then_inc(o_done, 1)

            def make_scores(t):
                pe.wait_ge(z_hi, t + 1)
                pe.wait_ge(z_lo, t + 1)
                nc.tensor.matmul(scores, ones_r[:, :], zs[:, :, :].rearrange("p h n -> p (h n)"),
                                 start=True, stop=True).then_inc(scores_done, 1)

            def tile(t, p, last=False):
                make_h(t, p, range(KC))
                rest(t, p, last)

            def rest(t, p, last=False):
                pe.wait_ge(out_ready, 2 * t)
                base(t, p, 0, range(HK))
                turn_g(t)
                base(t, p, 0, range(HK, KC))
                add_lora(t, 0)
                if not last:
                    make_y(t + 1, 0)
                base(t, p, 1, range(HK))
                if not last:
                    pe.wait_ge(y_added, YR * (t + 1) + 1)
                    make_y(t + 1, 1)
                base(t, p, 1, range(HK, KC))
                add_lora(t, 1)
                if not last:
                    make_scores(t + 1)

            def turn_org(n):
                at = place["org", n]
                pe.wait_ge(piece_loaded[at], 16)
                for j in range(2):
                    if 2 * n + j >= TB:
                        pe.wait_ge(org_lo, 2 * n + j - TB + 1)
                    for k in range(HK):
                        c = j * HK + k
                        mm = nc.tensor.transpose(turn_ps[(2 * n + j) % TB][:, k * P:(k + 1) * P],
                                                 chunk_cols(stage[at % RING], c), ident[:, :])
                    mm.then_inc(org_turned, 1)

            pe.wait_ge(ident_ready, 1)
            pe.wait_ge(keys_loaded, 16)
            nc.tensor.transpose(keys_ps, keys_sb[:, :], ident[0:E, 0:E]).then_inc(keys_turned, 1)
            make_y(0, 0)
            pe.wait_ge(y_added, 1)
            make_y(0, 1)
            pe.wait_ge(keys_ready, 1)
            at = place["wq", 0]
            pe.wait_ge(piece_loaded[at], 16)
            for k in range(KC):
                mm = nc.tensor.matmul(gate_ps[:, k, :], chunk_cols(stage[at % RING], k), keys_t[:, :],
                                      start=True, stop=True)
            mm.then_inc(gate_done, 1)
            turn_org(0)
            for n in range(DP):
                pe.wait_ge(down_hi, n + 1)
                pe.wait_ge(down_lo[n], 1)
            for n in range(1, OC // 2):
                make_h(0, 0, range(2 * n - 2, 2 * n))
                turn_org(n)
                if n == 1:
                    pe.wait_ge(ones_copied, 1)
                    make_scores(0)
            make_h(0, 0, range(OC - 2, KC))
            pe.wait_ge(org_hi, OC)
            pe.wait_ge(org_lo, OC)
            for n in range(OC // 2, OC):
                k = 2 * (n - OC // 2)
                turn_org(n)
                base(0, 0, 0, range(k, k + 2))
            pe.wait_ge(org_hi, 2 * OC)
            pe.wait_ge(org_lo, 2 * OC)
            turn_g(0)
            base(0, 0, 1, range(HK))
            make_y(1, 0)
            base(0, 0, 1, range(HK, KC))
            pe.wait_ge(y_added, YR + 1)
            make_y(1, 1)
            add_lora(0, 0, first=True)
            add_lora(0, 1)
            make_scores(1)
            with pe.Fori(0, T // 2 - 1) as i:
                for u in range(2):
                    tile(2 * i + (1 + u), (1 + u) % 2)
            tile(T - 1, 1, last=True)


_INS = ['x', 'itok_B_0_15', 'L0_cond_weights', 'L0_ffn_W_org', 'L0_ffn_lora_down', 'L0_ffn_lora_up',
        'L0_ffn_lora_keys', 'L0_ffn_Wq']


def kernel(**inputs):
    import numpy as _np
    import concourse.bacc as _bacc
    from concourse import mybir as _mybir
    from concourse.bass_utils import run_bass_kernel_spmd as _run

    nc = _bacc.Bacc("TRN2", target_bir_lowering=False, num_devices=1)
    arrays, args = {}, []
    for name in _INS:
        a = _np.ascontiguousarray(inputs[name])
        arrays[f"in_{name}_dram"] = a
        args.append(nc.dram_tensor(f"in_{name}_dram", a.shape, _mybir.dt.from_np(a.dtype), kind="ExternalInput").ap())
    shape = inputs['x'].shape
    args.append(nc.dram_tensor("out_0_dram", shape, _mybir.dt.float32, kind="ExternalOutput").ap())
    adaln_ffn(nc, *args)
    r = _run(nc, [arrays], core_ids=[0])
    return r.results[0]["out_0_dram"]
```
